# Optimizing a Trainium2 kernel written in Bass

```python
import numpy as np
import jax
import jax.numpy as jnp

def _softmax(x, axis=-1):
    return jax.nn.softmax(x, axis=axis)

def _gelu(x):
    return jax.nn.gelu(x, approximate=True)

def _silu(x):
    return jax.nn.silu(x)

def _sigmoid(x):
    return jax.nn.sigmoid(x)

def _layernorm(x, axis=-1, eps=1e-05):
    m = jnp.mean(x, axis=axis, keepdims=True)
    v = jnp.var(x, axis=axis, keepdims=True)
    return (x - m) / jnp.sqrt(v + eps)

def _scatter_add(tgt, idx, src, axis=0):
    return tgt.at[idx].add(src)

def _segment_sum(src, seg, n):
    return jax.ops.segment_sum(src, seg, n)
kernel_name = 'mk_adj_preln_d1_adj_r2_c952da'

def setup_inputs(seed: int=0):
    np.random.seed(seed)
    _w = jnp.asarray

    def _rec_inputs():
        import jax
        import jax.numpy as jnp
        _gk = jax.random.key(seed)
        x = -0.0001538 + 1 * jax.random.normal(jax.random.fold_in(_gk, 1), (128, 128, 384), jnp.float32)
        _a = jax.random.bernoulli(jax.random.fold_in(_gk, 2), 0.03125, (128, 128, 128))
        _a = jnp.logical_or(_a, jnp.swapaxes(_a, -1, -2))
        _a = jnp.logical_or(_a, jnp.eye(128, dtype=bool))
        _af = _a.astype(jnp.float32)
        _af = _af * jax.random.uniform(jax.random.fold_in(_gk, 3), (128, 128, 128), jnp.float32, 0.05, 0.999992)
        adj = _af
        return (x, adj)
    x, adj = _rec_inputs()

    def _L0_gnn_setup():
        import jax, jax.numpy as jnp
        import numpy as np
        B, N, D, H = (8, 512, 384, 12)
        HD = D // H

        def _split_heads(x):
            b, n, _ = x.shape
            return x.reshape(b, n, H, HD).transpose(0, 2, 1, 3)
        key = jax.random.key(seed)
        ks = jax.random.split(key, 10)
        input_graph = jax.random.normal(ks[0], (B, N, D), dtype=jnp.float32)
        u = jax.random.uniform(ks[1], (B, N, N), dtype=jnp.float32)
        keep = jax.random.uniform(ks[2], (B, N, N)) < 0.15
        adj = jnp.where(keep, u, 0.0)
        s = 1.0 / np.sqrt(D)
        Wq = jax.random.normal(ks[3], (D, D), dtype=jnp.float32) * s
        bq = jnp.zeros((D,), dtype=jnp.float32)
        Wk = jax.random.normal(ks[4], (D, D), dtype=jnp.float32) * s
        bk = jnp.zeros((D,), dtype=jnp.float32)
        Wv = jax.random.normal(ks[5], (D, D), dtype=jnp.float32) * s
        bv = jnp.zeros((D,), dtype=jnp.float32)
        beta = jnp.asarray(0.1, dtype=jnp.float32)
        return {'input_graph': input_graph, 'adj': adj, 'Wq': Wq, 'bq': bq, 'Wk': Wk, 'bk': bk, 'Wv': Wv, 'bv': bv, 'beta': beta}
    _L0_gnn_all = _L0_gnn_setup()
    _L0_gnn_in = {k: v for k, v in _L0_gnn_all.items() if k in ('Wq', 'bq', 'Wk', 'bk', 'Wv', 'bv', 'beta')}
    del _L0_gnn_all
    return {'x': x, 'adj': adj, 'L0_gnn_Wq': _L0_gnn_in['Wq'], 'L0_gnn_bq': _L0_gnn_in['bq'], 'L0_gnn_Wk': _L0_gnn_in['Wk'], 'L0_gnn_bk': _L0_gnn_in['bk'], 'L0_gnn_Wv': _L0_gnn_in['Wv'], 'L0_gnn_bv': _L0_gnn_in['bv'], 'L0_gnn_beta': _L0_gnn_in['beta']}

def reference(x, adj, L0_gnn_Wq, L0_gnn_bq, L0_gnn_Wk, L0_gnn_bk, L0_gnn_Wv, L0_gnn_bv, L0_gnn_beta):
    import jax
    import jax.numpy as jnp

    def _L0_gnn_ref(input_graph, adj, Wq, bq, Wk, bk, Wv, bv, beta):
        import jax, jax.numpy as jnp
        import numpy as np
        B, N, D, H = (8, 512, 384, 12)
        HD = D // H

        def _split_heads(x):
            b, n, _ = x.shape
            return x.reshape(b, n, H, HD).transpose(0, 2, 1, 3)
        q = _split_heads(input_graph @ Wq + bq)
        k = _split_heads(input_graph @ Wk + bk)
        v = _split_heads(input_graph @ Wv + bv)
        scores = jnp.einsum('bhqd,bhkd->bhqk', q, k) / jnp.sqrt(jnp.asarray(HD, input_graph.dtype))
        adj_e = adj[:, None, :, :]
        scores = scores + beta * adj_e
        scores = jnp.where(adj_e > 0, scores, jnp.asarray(-9000000000000000.0, scores.dtype))
        probs = jax.nn.softmax(scores, axis=-1)
        out = jnp.einsum('bhqk,bhkd->bhqd', probs, v)
        return out.transpose(0, 2, 1, 3).reshape(input_graph.shape[0], input_graph.shape[1], D)
    h = jnp.maximum(_layernorm(x, axis=-1), 0.0)
    x = x + _L0_gnn_ref(h, adj, L0_gnn_Wq, L0_gnn_bq, L0_gnn_Wk, L0_gnn_bk, L0_gnn_Wv, L0_gnn_bv, L0_gnn_beta)
    return x

_drawn_inputs = setup_inputs


def setup_inputs(seed=0):
    import zlib

    import numpy as np

    out = dict(_drawn_inputs(seed))
    spreads = {'L0_gnn_bq': (0.0, 0.744), 'L0_gnn_bk': (0.0, 0.8), 'L0_gnn_bv': (0.0, 0.1)}
    factors = {}
    for name, (base, spread) in spreads.items():
        noise = np.random.default_rng([zlib.crc32(name.encode()), seed]).standard_normal(out[name].shape)
        drawn = base * np.exp(spread * noise) if base else spread * noise
        out[name] = jnp.asarray(drawn.astype(out[name].dtype))
    for name, factor in factors.items():
        out[name] = (out[name] * factor).astype(out[name].dtype)
    return out
```

```python
from contextlib import ExitStack

import concourse.bass as bass
from concourse import mybir

F32 = mybir.dt.float32
F32R = mybir.dt.float32r
BF16 = mybir.dt.bfloat16
FP16 = mybir.dt.float16
ALU = mybir.AluOpType
ACT = mybir.ActivationFunctionType

HEADS = 12
EPS = 1e-5
MASKED = -9000000000000000.0


def graph_attention_kernel(nc, x, adj, wq, bq, wk, bk, wv, bv, beta, out):
    GRAPHS, N, D = x.shape
    P = 128
    HD = D // HEADS
    HPC = P // HD
    CH = D // P
    G = 4
    STEPS = GRAPHS // G
    TOK = G * N
    SLOTS = G * CH
    SCALE = float(HD) ** -0.5
    VW = HD + 1
    assert N == P and TOK == 512 and HPC * N == 512

    UNITS = ([("turn", c) for c in range(CH)] + [("k", c) for c in range(CH)]
             + [("q", c) for c in range(CH)] + [("v", j) for j in range(G)])
    NU = len(UNITS)
    SPLITS = 3 * CH
    UNITS_AT = [[0, 1], [2]] + [[k] for k in range(3, NU)]
    assert len(UNITS_AT) == SLOTS
    PARTS = ((0, 0), (1, 0), (0, 1))
    MMS = CH * len(PARTS)
    FIRST, ALL = (CH - 1) * len(PARTS), MMS * (NU - CH)
    ENDS = [0, 0] + [FIRST + (ALL - FIRST) * i // (SLOTS - 2) for i in range(SLOTS - 1)]
    PIECES = [[(CH + k, max(a, MMS * k) - MMS * k, min(b, MMS * (k + 1)) - MMS * k)
               for k in range(NU - CH) if max(a, MMS * k) < min(b, MMS * (k + 1))]
              for a, b in zip(ENDS, ENDS[1:])]
    assert all(k in UNITS_AT[u] for u in range(SLOTS) for k, _, b in PIECES[u] if b == MMS)

    x_v = x.rearrange("(s j) t d -> s t j d", j=G)
    adj_v = adj.rearrange("(s j) q k -> s q j k", j=G)
    out_v = out.rearrange("(s j) t d -> s j t d", j=G)

    with ExitStack() as ctx:
        def sb(name, shape, dt):
            return ctx.enter_context(nc.sbuf_tensor(name, shape, dt))

        def sem(name):
            return ctx.enter_context(nc.semaphore(name))

        w = sb("w", [P, 2, CH, 3 * D], F32R)
        ident = sb("ident", [P, P], F32)
        bias_qk = sb("bias_qk", [P, 2, CH], F32)
        bv_row = sb("bv_row", [P, D], F32)
        beta_col = sb("beta_col", [P, 1], F32)
        half = sb("half", [P, G], F32)
        xs = sb("xs", [P, 2, G, D], F32)
        adjs = sb("adjs", [P, G, N], F32)
        mask = sb("mask", [P, 2, G, N], F32)
        xb = sb("xb", [P, 2, G, D], F32)
        stats = sb("stats", [P, G, 6], F32)
        mean_var = sb("mean_var", [P, G, 2], F32)
        var_eps = sb("var_eps", [P, G], F32)
        rstd = sb("rstd", [P, G], F32)
        hn = sb("hn", [P, G, D], F32)
        hT = sb("hT", [P, 2, CH, TOK], F32R)
        qT = sb("qT", [P, 2, 2, CH, TOK], F32R)
        kT = sb("kT", [P, 2, CH, TOK], F32R)
        k_bd = sb("k_bd", [P, G, 2, CH, HPC, N], F32R)
        v1 = sb("v1", [P, 2, G, HEADS, VW], F32)
        v2 = sb("v2", [P, 2, G, HEADS, HD], F32)
        v3 = sb("v3", [P, 2, G, HEADS, HD], BF16)
        biased = sb("biased", [P, 2, HPC, N], F32)
        neg_max = sb("neg_max", [P, 2, HPC], F32)
        probs = sb("probs", [P, 2, HPC, N], F32)
        pT = sb("pT", [P, 2, 2, HPC, N], FP16)
        inv_sum = sb("inv_sum", [P, 2, HEADS], F32)
        on = sb("on", [P, 2, D], F32)

        ps_s = [ctx.enter_context(nc.psum_tensor(f"ps_s{b}", [P, 512], F32)) for b in range(2)]
        ps_t = [ctx.enter_context(nc.psum_tensor(f"ps_t{b}", [P, 512], F32)) for b in range(2)]
        ps_p = [ctx.enter_context(nc.psum_tensor(f"ps_p{b}", [P, 512], F32)) for b in range(2)]
        ps_o = [ctx.enter_context(nc.psum_tensor(f"ps_o{b}", [P, 512], F32)) for b in range(2)]

        weights_in = sem("weights_in")
        x_in = [sem(f"x_in{b}") for b in range(2)]
        adj_in = sem("adj_in")
        k_bd_in = [sem(f"k_bd_in{j}") for j in range(G)]
        stored = [sem(f"stored{b}") for b in range(2)]
        consts_set = sem("consts_set")
        k_bd_cleared = sem("k_bd_cleared")
        ident_zeroed = sem("ident_zeroed")
        w_high = sem("w_high")
        w_low = sem("w_low")
        stats_done = sem("stats_done")
        var_done = sem("var_done")
        eps_added = sem("eps_added")
        rstd_done = sem("rstd_done")
        normed = sem("normed")
        unlinked = sem("unlinked")
        mask_done = sem("mask_done")
        xb_done = sem("xb_done")
        proj_done = sem("proj_done")
        high_done = sem("high_done")
        low_done = sem("low_done")
        v_copied = sem("v_copied")
        v2_done = sem("v2_done")
        v3_done = sem("v3_done")
        scores_done = sem("scores_done")
        biased_done = sem("biased_done")
        exp_done = sem("exp_done")
        turned = sem("turned")
        p_high_done = sem("p_high_done")
        p_low_done = sem("p_low_done")
        pv_done = sem("pv_done")
        inverted = sem("inverted")
        scaled = sem("scaled")
        added = sem("added")

        def wait(eng, s, value):
            if not isinstance(value, int) or value > 0:
                eng.wait_ge(s, value)

        def upper(ap):
            return ap.bitcast(BF16).rearrange("p a (n two) -> p a n two", two=2)[:, :, :, 1]

        def run_steps(eng, step):
            step(0, 0)
            step(1, 1)
            with eng.Fori(1, STEPS // 2 - 1) as pair:
                step(2 * pair, 0, True)
                step(2 * pair + 1, 1, True)
            step(STEPS - 2, 0)
            step(STEPS - 1, 1)
            step(STEPS, 0)

        def has(s, looped, first, last):
            return looped or first <= s <= last

        block = ctx.enter_context(nc.Block())

        @block.sync
        def _(sp):
            wv_stage = hn[:, 0:CH, :]
            for n, src in enumerate((wq, wk)):
                sp.dma_start(xb[:, n, 0:CH, :], src.rearrange("(c p) n -> p c n", p=P)).then_inc(weights_in, 16)
            sp.dma_start(wv_stage, wv.rearrange("(c p) n -> p c n", p=P)).then_inc(weights_in, 16)
            for n, src in enumerate((bq, bk)):
                sp.dma_start(bias_qk[:, n, :], src.rearrange("(c p) -> p c", p=P),
                             allow_slow_non_contiguous=True).then_inc(weights_in, 16)
            sp.dma_start(bv_row[:], bv.rearrange("(o d) -> o d", o=1).broadcast_to([P, D])).then_inc(weights_in, 16)
            sp.dma_start(beta_col[:], beta.broadcast_to([P, 1])).then_inc(weights_in, 16)
            sp.dma_start(xs[:, 0], x_v[0]).then_inc(x_in[0], 16)
            sp.dma_start(adjs[:], adj_v[0]).then_inc(adj_in, 16)
            sp.dma_start(xs[:, 1], x_v[1]).then_inc(x_in[1], 16)

            def spread_k(s, j):
                wait(sp, low_done, SPLITS * s + 2 * CH)
                sp.nop(nofuse=True)
                wait(sp, scores_done, SLOTS * (s - 1) + CH * (j + 1))
                sp.nop(nofuse=True)
                for i in range(HPC):
                    rows = slice(HD * i, HD * (i + 1))
                    sp.dma_start(k_bd[rows, j, :, :, i, :].bitcast(F32),
                                 kT[rows, :, :, j * N:(j + 1) * N].bitcast(F32)).then_inc(k_bd_in[j], 16)

            def store(s, j):
                wait(sp, added, G * (s - 1) + j + 1)
                sp.nop(nofuse=True)
                sp.dma_start(out_v[s - 1, j], on[:, j % 2, :]).then_inc(stored[j % 2], 16)

            sp.wait_ge(k_bd_cleared, G)

            def step(s, par, looped=False):
                if has(s, looped, 0, STEPS - 1):
                    spread_k(s, 0)
                if has(s, looped, 1, STEPS):
                    store(s, 0)
                if has(s, looped, 0, STEPS - 1):
                    spread_k(s, 1)
                if has(s, looped, 1, STEPS):
                    store(s, 1)
                if has(s, looped, 0, STEPS - 1):
                    spread_k(s, 2)
                if has(s, looped, 0, STEPS - 3):
                    sp.wait_ge(xb_done, G * (s + 1))
                    sp.wait_ge(normed, G * (s + 1))
                    sp.nop(nofuse=True)
                    sp.dma_start(xs[:, par], x_v[s + 2]).then_inc(x_in[par], 16)
                if has(s, looped, 1, STEPS):
                    store(s, 2)
                if has(s, looped, 0, STEPS - 1):
                    spread_k(s, 3)
                if has(s, looped, 0, STEPS - 2):
                    sp.wait_ge(mask_done, s + 1)
                    sp.nop(nofuse=True)
                    sp.dma_start(adjs[:], adj_v[s + 1]).then_inc(adj_in, 16)
                if has(s, looped, 1, STEPS):
                    store(s, 3)

            run_steps(sp, step)
            for b in range(2):
                sp.wait_ge(stored[b], 16 * GRAPHS // 2)

        @block.gpsimd
        def _(pool):
            pool.memset(ident[:], 0.0).then_inc(ident_zeroed, 1)
            pool.wait_ge(ident_zeroed, 1)
            pool.affine_select(out=ident[:], in_=ident[:], compare_op=ALU.not_equal, fill=1.0, base=0,
                               pattern=[[-1, P]], channel_multiplier=1).then_inc(consts_set, 1)
            pool.memset(half[:], -0.5).then_inc(consts_set, 1)

            def rstd_of(s):
                wait(pool, var_done, G * (s + 1))
                wait(pool, rstd_done, s)
                pool.nop(nofuse=True)
                pool.tensor_scalar(var_eps[:], mean_var[:, :, 1], EPS, None, ALU.add).then_inc(eps_added, 1)
                pool.wait_ge(eps_added, s + 1)
                wait(pool, normed, G * s)
                pool.tensor_tensor(rstd[:], var_eps[:], half[:], ALU.pow).then_inc(rstd_done, 1)

            def add_bias(s, par, j):
                wait(pool, x_in[par], 8 * (s - par) + 16)
                wait(pool, added, G * (s - 2) + j + 1)
                pool.tensor_tensor(xb[:, par, j, :], xs[:, par, j, :], bv_row[:], ALU.add).then_inc(xb_done, 1)

            def split_v(s, par, j):
                pool.wait_ge(v_copied, G * s + j + 1)
                pool.tensor_tensor(v2[:, par, j], v1[:, par, j, :, 0:HD], upper(v1[:, par, j])[:, :, 0:HD],
                                   ALU.subtract).then_inc(v2_done, 1)
                pool.wait_ge(v2_done, G * s + j + 1)
                pool.tensor_tensor(v3[:, par, j], v2[:, par, j], upper(v2[:, par, j]),
                                   ALU.subtract).then_inc(v3_done, 1)

            def add_x(s, par, j):
                pool.wait_ge(scaled, G * (s - 1) + j + 1)
                pool.wait_ge(xb_done, G * (s - 1) + j + 1)
                pool.tensor_tensor(on[:, j % 2, :], on[:, j % 2, :], xb[:, 1 - par, j, :], ALU.add).then_inc(added, 1)

            def step(s, par, looped=False):
                proj, attend = has(s, looped, 0, STEPS - 1), has(s, looped, 1, STEPS)
                for j in range(G):
                    if proj:
                        add_bias(s, par, j)
                    if j == 1 and has(s, looped, 0, STEPS - 2):
                        rstd_of(s + 1)
                    if attend and j < G - 1:
                        add_x(s, par, j)
                if proj:
                    for j in range(G):
                        split_v(s, par, j)
                if attend:
                    add_x(s, par, G - 1)

            pool.wait_ge(weights_in, 16 * 7)
            pool.wait_ge(consts_set, 2)
            rstd_of(0)
            for j in range(G):
                pool.memset(k_bd[:, j:j + 1].bitcast(F32), 0.0).then_inc(k_bd_cleared, 1)
            pool.wait_ge(w_low, 3)
            run_steps(pool, step)

        @block.tensor
        def _(pe):
            def bank_free(s, k):
                before, last = (s, k - 2) if k >= 2 else (s - 1, k - 2 + NU)
                if last < SPLITS:
                    wait(pe, low_done, SPLITS * before + last + 1)
                else:
                    wait(pe, v_copied, G * before + last - SPLITS + 1)

            def turn(s, par, k):
                bank, c = ps_p[(par + k) % 2], UNITS[k][1]
                bank_free(s, k)
                pe.wait_ge(normed, G * (s + 1))
                for j in range(G):
                    mm = pe.transpose(bank[:, j * N:(j + 1) * N], hn[:, j, c * P:(c + 1) * P], ident[:])
                mm.then_inc(proj_done, 1)

            def project(s, par, k, first, end):
                kind, n = UNITS[k]
                bank = ps_p[(par + k) % 2]
                if first == 0:
                    bank_free(s, k)
                for m in range(first, end):
                    c, (a, b) = m // len(PARTS), PARTS[m % len(PARTS)]
                    if k == CH and m % len(PARTS) == 0:
                        pe.wait_ge(low_done, SPLITS * s + c + 1)
                    if kind == "v":
                        dst, stationary, moving = bank[:, 0:D], hT[:, a, c, n * N:(n + 1) * N], w[:, b, c, 2 * D:3 * D]
                    else:
                        col = (D if kind == "k" else 0) + n * P
                        dst, stationary, moving = bank[:], w[:, a, c, col:col + P], hT[:, b, c, :]
                    mm = pe.matmul(dst, stationary, moving, start=m == 0, stop=m == MMS - 1)
                if end == MMS:
                    mm.then_inc(proj_done, 1)

            def scores(s, par, u):
                j, c, n = u // CH, u % CH, SLOTS * (s - 1) + u
                if c == 0:
                    pe.wait_ge(k_bd_in[j], 16 * HPC * s)
                if u == 0:
                    pe.wait_ge(low_done, SPLITS * s)
                wait(pe, biased_done, HPC * (n - 1))
                for a, b in PARTS:
                    mm = pe.matmul(ps_s[u % 2][:], qT[:, 1 - par, a, c, j * N:(j + 1) * N], k_bd[:, j, b, c],
                                   start=(a, b) == (0, 0), stop=(a, b) == PARTS[-1])
                mm.then_inc(scores_done, 1)

            def turn_probs(n, odd):
                pe.wait_ge(exp_done, HPC * (n + 1))
                wait(pe, p_low_done, n - 1)
                for i in range(HPC):
                    mm = pe.transpose(ps_t[odd][:, i * N:(i + 1) * N], probs[:, odd, i, :], ident[:])
                mm.then_inc(turned, 1)

            def values_of(s, par, late, j, c, n, odd):
                vp = par if late else 1 - par
                pe.wait_ge(p_low_done, n + 1)
                for i in range(HPC):
                    h = c * HPC + i
                    o = ps_o[j % 2][:, h * VW:(h + 1) * VW]
                    high, low = pT[:, odd, 0, i, :], pT[:, odd, 1, i, :]
                    first, second = upper(v1[:, vp, j])[:, h, :], upper(v2[:, vp, j])[:, h, :]
                    third = v3[:, vp, j, h, :]
                    pe.matmul(o, high, first, start=True, stop=False)
                    pe.matmul(o, low, first, start=False, stop=False)
                    pe.matmul(o[:, 0:HD], high, second, start=False, stop=False)
                    pe.matmul(o[:, 0:HD], low, second, start=False, stop=False)
                    mm = pe.matmul(o[:, 0:HD], high, third, start=False, stop=True)
                mm.then_inc(pv_done, 1)

            def step(s, par, looped=False):
                proj, attend = has(s, looped, 0, STEPS - 1), has(s, looped, 1, STEPS)
                drain = not looped and s == STEPS
                for u in range(SLOTS + drain):
                    n = SLOTS * (s - 1) + u
                    behind = attend and (looped or n >= 1)
                    if attend and u < SLOTS:
                        scores(s, par, u)
                    if behind:
                        turn_probs(n - 1, (u - 1) % 2)
                    if proj:
                        for k in UNITS_AT[u]:
                            if k < CH:
                                turn(s, par, k)
                        for k, first, end in PIECES[u]:
                            project(s, par, k, first, end)
                    if behind:
                        late = u < 1
                        v = (u - 1) % SLOTS
                        j, c = v // CH, v % CH
                        if c == 0:
                            g = G * (s - 1 - late) + j
                            wait(pe, scaled, g - 1)
                            pe.wait_ge(v3_done, g + 1)
                        values_of(s, par, late, j, c, n - 1, (u - 1) % 2)

            pe.wait_ge(consts_set, 2)
            pe.wait_ge(w_low, 3)
            run_steps(pe, step)

        @block.scalar
        def _(act):
            act.wait_ge(weights_in, 16 * 7)
            for n, (src, scale) in enumerate(((xb[:, 0, 0:CH, :], SCALE), (xb[:, 1, 0:CH, :], 1.0), (hn[:, 0:CH, :], 1.0))):
                act.activation(w[:, 0, :, n * D:(n + 1) * D], src, ACT.Copy, scale=scale).then_inc(w_high, 1)

            def exps(s, u):
                n, odd = SLOTS * (s - 1) + u, u % 2
                wait(act, turned, n - 1)
                for i in range(HPC):
                    act.wait_ge(biased_done, HPC * n + i + 1)
                    act.activation(probs[:, odd, i, :], biased[:, odd, i, :], ACT.Exp,
                                   bias=neg_max[:, odd, i:i + 1], scale=-1.0).then_inc(exp_done, 1)

            def high_part(s, par, k):
                kind, n = UNITS[k]
                bank = ps_p[(par + k) % 2]
                act.wait_ge(proj_done, NU * s + k + 1)
                if kind == "turn":
                    act.activation(hT[:, 0, n, :], bank[:], ACT.Relu).then_inc(high_done, 1)
                elif kind == "k":
                    if n == 0:
                        for j in range(G):
                            wait(act, k_bd_in[j], 16 * HPC * s)
                    act.activation(kT[:, 0, n, :], bank[:], ACT.Identity, bias=bias_qk[:, 1, n:n + 1]).then_inc(high_done, 1)
                elif kind == "q":
                    if n == 0:
                        wait(act, scores_done, SLOTS * (s - 1))
                    act.activation(qT[:, par, 0, n, :], bank[:], ACT.Identity, bias=bias_qk[:, 0, n:n + 1]).then_inc(high_done, 1)
                else:
                    wait(act, pv_done, SLOTS * (s - 2) + CH * (n + 1))
                    act.activation(v1[:, par, n, :, 0:HD], bank[:, 0:D].rearrange("p (h d) -> p h d", d=HD),
                                   ACT.Copy).then_inc(v_copied, 1)

            def p_high(n, odd):
                act.wait_ge(turned, n + 1)
                wait(act, pv_done, n - 1)
                act.activation(pT[:, odd, 0], ps_t[odd][:].rearrange("p (h q) -> p h q", q=N),
                               ACT.Copy).then_inc(p_high_done, 1)

            def step(s, par, looped=False):
                proj, attend = has(s, looped, 0, STEPS - 1), has(s, looped, 1, STEPS)
                drain = not looped and s == STEPS
                for u in range(SLOTS + drain):
                    n = SLOTS * (s - 1) + u
                    if attend and (looped or n >= 1):
                        p_high(n - 1, (u - 1) % 2)
                    if attend and u < SLOTS:
                        exps(s, u)
                    if proj:
                        for k in UNITS_AT[u]:
                            high_part(s, par, k)

            act.wait_ge(consts_set, 3)
            run_steps(act, step)

        @block.vector
        def _(dve):
            dve.memset(v1[:, :, :, :, HD:VW], 1.0)
            dve.wait_ge(weights_in, 16 * 7)
            dve.tensor_scalar(bias_qk[:, 0, :], bias_qk[:, 0, :], SCALE, None, ALU.mult).then_inc(consts_set, 1)
            for n, (src, scale) in enumerate(((xb[:, 0, 0:CH, :], SCALE), (xb[:, 1, 0:CH, :], 1.0), (hn[:, 0:CH, :], 1.0))):
                dve.wait_ge(w_high, n + 1)
                cols = slice(n * D, (n + 1) * D)
                dve.scalar_tensor_tensor(out=w[:, 1, :, cols], in0=src, scalar=scale, in1=w[:, 0, :, cols].bitcast(F32),
                                         op0=ALU.mult, op1=ALU.subtract).then_inc(w_low, 1)

            def moments(s, par, j):
                wait(dve, x_in[par], 8 * (s - par) + 16)
                wait(dve, var_done, G * (s - 1) + j + 1)
                dve.bn_stats(stats[:, j, :], xs[:, par, j, :]).then_inc(stats_done, 1)

            def variance(s, j):
                wait(dve, rstd_done, s)
                wait(dve, normed, G * (s - 1) + j + 1)
                dve.wait_ge(stats_done, G * s + j + 1)
                dve.nop(nofuse=True)
                dve.bn_aggr(mean_var[:, j, :], stats[:, j, :]).then_inc(var_done, 1)

            def normalise(s, par, j):
                dve.wait_ge(rstd_done, s + 1)
                wait(dve, proj_done, NU * (s - 1) + CH)
                dve.tensor_scalar(hn[:, j, :], xs[:, par, j, :], mean_var[:, j, 0:1], rstd[:, j:j + 1],
                                  ALU.subtract, ALU.mult).then_inc(normed, 1)

            def mask_unlinked(s, par):
                dve.wait_ge(adj_in, 16 * (s + 1))
                wait(dve, biased_done, HPC * SLOTS * (s - 1))
                dve.tensor_scalar(mask[:, par], adjs[:], 0.0, MASKED, ALU.is_le, ALU.mult).then_inc(unlinked, 1)

            def mask_linked(s, par):
                dve.wait_ge(unlinked, s + 1)
                dve.scalar_tensor_tensor(out=mask[:, par], in0=adjs[:], scalar=beta_col[:, 0:1], in1=mask[:, par],
                                         op0=ALU.mult, op1=ALU.add).then_inc(mask_done, 1)

            def low_part(s, par, k):
                kind, n = UNITS[k]
                bank = ps_p[(par + k) % 2][:]
                dve.wait_ge(high_done, SPLITS * s + k + 1)
                if kind == "turn":
                    dve.scalar_tensor_tensor(out=hT[:, 1, n, :], in0=bank, scalar=0.0, in1=hT[:, 0, n, :].bitcast(F32),
                                             op0=ALU.max, op1=ALU.subtract).then_inc(low_done, 1)
                    return
                dst, b = (kT[:, :, n, :], bias_qk[:, 1, n:n + 1]) if kind == "k" else (qT[:, par, :, n, :], bias_qk[:, 0, n:n + 1])
                dve.scalar_tensor_tensor(out=dst[:, 1, :], in0=bank, scalar=b, in1=dst[:, 0, :].bitcast(F32),
                                         op0=ALU.add, op1=ALU.subtract).then_inc(low_done, 1)

            def bias_scores(s, par, u):
                n, odd = SLOTS * (s - 1) + u, u % 2
                dve.wait_ge(scores_done, n + 1)
                wait(dve, exp_done, HPC * (n - 1))
                if u == 0:
                    dve.wait_ge(mask_done, s)
                dve.nop(nofuse=True)
                for i in range(HPC):
                    dve.tensor_tensor_reduce(out=biased[:, odd, i, :], in0=ps_s[odd][:, i * N:(i + 1) * N],
                                             in1=mask[:, 1 - par, u // CH, :], scale=-1.0, scalar=3.0e38, op0=ALU.add,
                                             op1=ALU.min, accum_out=neg_max[:, odd, i:i + 1]).then_inc(biased_done, 1)

            def p_low(n, odd):
                dve.wait_ge(p_high_done, n + 1)
                dve.tensor_tensor(pT[:, odd, 1], ps_t[odd][:].rearrange("p (h q) -> p h q", q=N), pT[:, odd, 0],
                                  ALU.subtract).then_inc(p_low_done, 1)

            def outputs(j):
                return ps_o[j % 2][:, 0:HEADS * VW].rearrange("p (h d) -> p h d", d=VW)

            def invert_sums(s, late, j):
                g = G * (s - 1 - late) + j
                dve.wait_ge(pv_done, CH * (g + 1))
                wait(dve, scaled, g - 1)
                dve.reciprocal(inv_sum[:, j % 2, :], outputs(j)[:, :, HD]).then_inc(inverted, 1)

            def scale_out(s, late, j):
                g = G * (s - 1 - late) + j
                dve.wait_ge(inverted, g + 1)
                wait(dve, stored[j % 2], 16 * (G // 2 * (s - 1 - late) + j // 2))
                dve.tensor_tensor(on[:, j % 2, :].rearrange("p (h d) -> p h d", d=HD), outputs(j)[:, :, 0:HD],
                                  inv_sum[:, j % 2, :].rearrange("p (h o) -> p h o", o=1).broadcast_to([P, HEADS, HD]),
                                  ALU.mult).then_inc(scaled, 1)

            def step(s, par, looped=False):
                proj, attend = has(s, looped, 0, STEPS - 1), has(s, looped, 1, STEPS)
                ahead = has(s, looped, 0, STEPS - 2)
                drain = not looped and s == STEPS
                for u in range(SLOTS + 3 * drain):
                    n = SLOTS * (s - 1) + u
                    ended, j = attend and u % CH == 2 and (looped or n > CH), (u // CH - 1) % G
                    if attend and u < SLOTS:
                        bias_scores(s, par, u)
                    if attend and (looped or n >= 1) and u - 1 < SLOTS:
                        p_low(n - 1, (u - 1) % 2)
                    if proj and u == 6:
                        mask_unlinked(s, par)
                    if ended:
                        invert_sums(s, u < CH, j)
                    if ahead and 2 <= u < 2 + G:
                        moments(s + 1, 1 - par, u - 2)
                    if ahead and 7 <= u < 7 + G:
                        normalise(s + 1, 1 - par, u - 7)
                    if proj and u == 11:
                        mask_linked(s, par)
                    if ended:
                        scale_out(s, u < CH, j)
                    if ahead and 2 <= u < 2 + G:
                        variance(s + 1, u - 2)
                    if proj:
                        for k in UNITS_AT[u]:
                            if k < SPLITS:
                                low_part(s, par, k)

            for j in range(G):
                moments(0, 0, j)
                variance(0, j)
            dve.wait_ge(w_low, 3)
            for j in range(G):
                normalise(0, 0, j)
            run_steps(dve, step)


_INS = ["x", "adj", "L0_gnn_Wq", "L0_gnn_bq", "L0_gnn_Wk", "L0_gnn_bk", "L0_gnn_Wv", "L0_gnn_bv", "L0_gnn_beta"]


def kernel(**inputs):
    import numpy as np
    import concourse.bacc as bacc
    from concourse.bass_utils import run_bass_kernel_spmd

    nc = bacc.Bacc("TRN2", target_bir_lowering=False, num_devices=1)
    arrays, args = {}, []
    for name in _INS:
        a = np.ascontiguousarray(inputs[name])
        if a.ndim == 0:
            a = a.reshape(1, 1)
        arrays[f"in_{name}"] = a
        args.append(nc.dram_tensor(f"in_{name}", a.shape, mybir.dt.from_np(a.dtype), kind="ExternalInput").ap())
    shape = arrays["in_x"].shape
    args.append(nc.dram_tensor("out", shape, F32, kind="ExternalOutput").ap())
    graph_attention_kernel(nc, *args)
    return run_bass_kernel_spmd(nc, [arrays], core_ids=[0]).results[0]["out"]
```
